# Optimizing a Trainium2 kernel written in Bass

```python
import numpy as np
import jax
import jax.numpy as jnp

def _softmax(x, axis=-1):
    return jax.nn.softmax(x, axis=axis)

def _gelu(x):
    return jax.nn.gelu(x, approximate=True)

def _silu(x):
    return jax.nn.silu(x)

def _sigmoid(x):
    return jax.nn.sigmoid(x)

def _layernorm(x, axis=-1, eps=1e-05):
    m = jnp.mean(x, axis=axis, keepdims=True)
    v = jnp.var(x, axis=axis, keepdims=True)
    return (x - m) / jnp.sqrt(v + eps)

def _scatter_add(tgt, idx, src, axis=0):
    return tgt.at[idx].add(src)

def _segment_sum(src, seg, n):
    return jax.ops.segment_sum(src, seg, n)
kernel_name = 'mk_rec_standalone_d1_rec_r8_d3ff70'

def setup_inputs(seed: int=0):
    np.random.seed(seed)
    _w = jnp.asarray

    def _rec_inputs():
        import jax
        import jax.numpy as jnp
        _rk = jax.random.key(seed)
        r_sae_features = jax.random.uniform(jax.random.fold_in(_rk, 1), (1024, 2048), jnp.float32, 0.0, 1)
        return r_sae_features
    r_sae_features = _rec_inputs()

    def _L0_rec_setup():
        import jax, jax.numpy as jnp
        import numpy as np
        B, N, D, O = (1024, 2048, 512, 512)
        key = jax.random.key(seed)
        ks = jax.random.split(key, 8)
        s = lambda k, shape, scale: jax.random.normal(k, shape, dtype=jnp.float32) * scale
        return {'sae_features': jax.random.uniform(ks[0], (B, N), dtype=jnp.float32), 'emb': s(ks[1], (N, D), 0.02), 'linear_w': s(ks[2], (O, N), 0.01), 'linear_b': s(ks[3], (O,), 0.01), 'mlp1_w': s(ks[4], (D, D), 0.04), 'mlp1_b': s(ks[5], (D,), 0.01), 'mlp2_w': s(ks[6], (O, D), 0.04), 'mlp2_b': s(ks[7], (O,), 0.01)}
    _L0_rec_all = _L0_rec_setup()
    _L0_rec_in = {k: v for k, v in _L0_rec_all.items() if k in ('emb', 'linear_w', 'linear_b', 'mlp1_w', 'mlp1_b', 'mlp2_w', 'mlp2_b')}
    del _L0_rec_all
    return {'r_sae_features': r_sae_features, 'L0_rec_emb': _L0_rec_in['emb'], 'L0_rec_linear_w': _L0_rec_in['linear_w'], 'L0_rec_linear_b': _L0_rec_in['linear_b'], 'L0_rec_mlp1_w': _L0_rec_in['mlp1_w'], 'L0_rec_mlp1_b': _L0_rec_in['mlp1_b'], 'L0_rec_mlp2_w': _L0_rec_in['mlp2_w'], 'L0_rec_mlp2_b': _L0_rec_in['mlp2_b']}

def reference(r_sae_features, L0_rec_emb, L0_rec_linear_w, L0_rec_linear_b, L0_rec_mlp1_w, L0_rec_mlp1_b, L0_rec_mlp2_w, L0_rec_mlp2_b):
    import jax
    import jax.numpy as jnp

    def _L0_rec_ref(sae_features, emb, linear_w, linear_b, mlp1_w, mlp1_b, mlp2_w, mlp2_b):
        import jax, jax.numpy as jnp
        import numpy as np
        B, N, D, O = (1024, 2048, 512, 512)
        sum_emb = sae_features @ emb
        sum_sq = sae_features * sae_features @ (emb * emb)
        interaction = 0.5 * (sum_emb * sum_emb - sum_sq)
        h = jax.nn.relu(interaction @ mlp1_w.T + mlp1_b)
        interaction_out = h @ mlp2_w.T + mlp2_b
        linear_out = sae_features @ linear_w.T + linear_b
        return linear_out + interaction_out
    y = _L0_rec_ref(r_sae_features, L0_rec_emb, L0_rec_linear_w, L0_rec_linear_b, L0_rec_mlp1_w, L0_rec_mlp1_b, L0_rec_mlp2_w, L0_rec_mlp2_b)
    return y

_drawn_inputs = setup_inputs


def setup_inputs(seed=0):
    import zlib

    import numpy as np

    out = dict(_drawn_inputs(seed))
    spreads = {}
    factors = {}
    for name, (base, spread) in spreads.items():
        noise = np.random.default_rng([zlib.crc32(name.encode()), seed]).standard_normal(out[name].shape)
        drawn = base * np.exp(spread * noise) if base else spread * noise
        out[name] = jnp.asarray(drawn.astype(out[name].dtype))
    for name, factor in factors.items():
        out[name] = (out[name] * factor).astype(out[name].dtype)
    return out
```

```python
from contextlib import ExitStack

import concourse.bass as bass
from concourse import mybir

F32 = mybir.dt.float32
F32R = mybir.dt.float32r
ALU = mybir.AluOpType
ACT = mybir.ActivationFunctionType

P = 128
EMB, LIN, SQ = range(3)


def build(nc, xT, emb, linT, w1T, w2T, bias, outT):
    KT, _, B = xT.shape
    D = emb.shape[2]
    DT = D // P
    NB = 512
    H = B // NB
    BANKS = DT * H
    assert BANKS == 8 and H == 2 and KT % 2 == 0 and KT >= 16

    W1_AT, W2_AT, HID_AT, U_AT = 0, DT, 2 * DT, 2 * DT + BANKS

    with ExitStack() as ctx:
        def sb(name, shape, dt=F32):
            return ctx.enter_context(nc.sbuf_tensor(name, shape, dt))

        def sem(name):
            return ctx.enter_context(nc.semaphore(name))

        mov_hi = sb("mov_hi", [P, H * KT, NB], F32R)
        mov_lo = sb("mov_lo", [P, H * KT, NB], F32R)
        sta_hi = sb("sta_hi", [P, 2, D], F32R)
        sta_lo = sb("sta_lo", [P, 2, D], F32R)
        mov_raw = sb("mov_raw", [P, 2, B])
        sta_raw = sb("sta_raw", [P, 2, D])
        mov_sq = sb("mov_sq", [P, 2, B])
        sta_sq = sb("sta_sq", [P, 2, D])
        w_raw = sb("w_raw", [P, DT, D])
        act = sb("act", [P, BANKS, NB])
        lin = sb("lin", [P, BANKS, NB])
        b_sb = sb("b_sb", [P, 3, DT])
        psum = ctx.enter_context(nc.psum_tensor("psum", [P, BANKS, NB], F32))

        sta_loaded = [sem(f"sta_loaded{i}") for i in range(2)]
        mov_loaded = [sem(f"mov_loaded{i}") for i in range(2)]
        w1_loaded = sem("w1_loaded")
        w2_loaded = sem("w2_loaded")
        b_loaded = sem("b_loaded")
        sta_hi_ready = sem("sta_hi_ready")
        sta_lo_ready = sem("sta_lo_ready")
        tile_done = sem("tile_done")
        x_hi_ready = sem("x_hi_ready")
        x_lo_ready = sem("x_lo_ready")
        x2_ready = sem("x2_ready")
        x2_hi_ready = sem("x2_hi_ready")
        x2_lo_ready = sem("x2_lo_ready")
        e2_ready = sem("e2_ready")
        s_summed = sem("s_summed")
        s_evicted = sem("s_evicted")
        lin_summed = sem("lin_summed")
        lin_evicted = sem("lin_evicted")
        q_summed = sem("q_summed")
        u_ready = sem("u_ready")
        u_hi_ready = sem("u_hi_ready")
        u_lo_ready = sem("u_lo_ready")
        mlp1_summed = sem("mlp1_summed")
        hid_ready = sem("hid_ready")
        hid_hi_ready = sem("hid_hi_ready")
        hid_lo_ready = sem("hid_lo_ready")
        mlp2_summed = sem("mlp2_summed")
        y_ready = sem("y_ready")
        w1_hi_ready = sem("w1_hi_ready")
        w1_lo_ready = sem("w1_lo_ready")
        w2_hi_ready = sem("w2_hi_ready")
        w2_lo_ready = sem("w2_lo_ready")
        stored = sem("stored")

        def pair(ap, k):
            return ap[:, bass.ds(k * H, H), :]

        def loads(k, slot):
            return (k - slot) * 8 + 16

        block = ctx.enter_context(nc.Block())

        @block.sync
        def _(sp):
            def load_sta(src, k, slot, wait=None):
                if wait is not None:
                    sp.wait_ge(sta_lo_ready, wait)
                sp.dma_start(sta_raw[:, slot, :], src[bass.ds(k, 1), :, :].rearrange("a p n -> p (a n)")
                             ).then_inc(sta_loaded[slot], 16)

            def load_mov(k, slot, free=None, wait=None):
                if free is not None:
                    sp.wait_ge(free, wait)
                sp.dma_start(mov_raw[:, slot, :], xT[bass.ds(k, 1), :, :].rearrange("a p n -> p (a n)")
                             ).then_inc(mov_loaded[slot], 16)

            for k in range(2):
                load_sta(emb, k, k)
                load_mov(k, k)
            sp.dma_start(b_sb[:], bias).then_inc(b_loaded, 16)
            with sp.Fori(1, KT // 2) as pair_no:
                k0 = pair_no * 2
                for i in range(2):
                    load_sta(emb, k0 + i, i, k0 + i - 1)
                    load_mov(k0 + i, i, x_lo_ready, k0 + i - 1)
            with sp.Fori(0, KT // 2) as pair_no:
                k0 = pair_no * 2
                for i in range(2):
                    load_sta(linT, k0 + i, i, k0 + i + KT - 1)
            sp.dma_start(w_raw[:], w1T.rearrange("t p n -> p t n")).then_inc(w1_loaded, 16)
            for k in range(2):
                load_mov(k, k, x_lo_ready, KT + k - 1)
                load_sta(emb, k, k, 2 * KT + k - 1)
            with sp.Fori(1, KT // 2) as pair_no:
                k0 = pair_no * 2
                for i in range(2):
                    load_mov(k0 + i, i, x2_lo_ready, k0 + i - 1)
                    load_sta(emb, k0 + i, i, k0 + i + 2 * KT - 1)
            sp.wait_ge(w1_lo_ready, 1)
            sp.dma_start(w_raw[:], w2T.rearrange("t p n -> p t n")).then_inc(w2_loaded, 16)
            for j in range(BANKS):
                h, o = divmod(j, DT)
                sp.wait_ge(y_ready, j + 1)
                sp.dma_start(outT[o, :, h * NB:(h + 1) * NB], lin[:, j, :]).then_inc(stored, 16)
            sp.wait_ge(stored, 16 * BANKS)

        @block.tensor
        def _(pe):
            def product(bank, d, sta, slot, mov, at, start, stop):
                return nc.tensor.matmul(psum[:, bank, :], sta[:, slot, d * P:(d + 1) * P],
                                        mov[:, bass.ds(at, 1), :].rearrange("p a n -> p (a n)"),
                                        start=start, stop=stop)

            def use_tile(p, k, slot, mov_hi_sem, mov_lo_sem, first=False, last=False, evicted=None, summed=None):
                pe.wait_ge(sta_hi_ready, k + (p * KT + 1))
                pe.wait_ge(mov_hi_sem, k + 1)
                pe.wait_ge(mov_lo_sem, k + 1)
                pe.wait_ge(sta_lo_ready, k + (p * KT + 1))
                for d in range(DT):
                    if evicted is not None:
                        pe.wait_ge(evicted, H * (d + 1))
                    for h in range(H):
                        product(h * DT + d, d, sta_hi, slot, mov_hi, k * H + h, first, False)
                        product(h * DT + d, d, sta_hi, slot, mov_lo, k * H + h, False, False)
                    for h in range(H):
                        mm = product(h * DT + d, d, sta_lo, slot, mov_hi, k * H + h, False, last)
                        if h == H - 1 and d == DT - 1:
                            mm.then_inc(tile_done, 1)
                        if summed is not None and (h, d) != (H - 1, DT - 1):
                            mm.then_inc(summed, 1)

            pe.wait_ge(sta_hi_ready, 1)
            pe.wait_ge(x_hi_ready, 1)
            for d in range(DT):
                for h in range(H):
                    product(h * DT + d, d, sta_hi, 0, mov_hi, h, True, False)
            pe.wait_ge(sta_lo_ready, 1)
            for d in range(DT):
                for h in range(H):
                    product(h * DT + d, d, sta_lo, 0, mov_hi, h, False, False)
            pe.wait_ge(x_lo_ready, 1)
            for d in range(DT):
                for h in range(H):
                    mm = product(h * DT + d, d, sta_hi, 0, mov_lo, h, False, False)
            mm.then_inc(tile_done, 1)
            use_tile(EMB, 1, 1, x_hi_ready, x_lo_ready)
            with pe.Fori(1, KT // 2 - 1) as pair_no:
                k0 = pair_no * 2
                for i in range(2):
                    use_tile(EMB, k0 + i, i, x_hi_ready, x_lo_ready)
            use_tile(EMB, KT - 2, 0, x_hi_ready, x_lo_ready)
            use_tile(EMB, KT - 1, 1, x_hi_ready, x_lo_ready, last=True, summed=s_summed)

            use_tile(LIN, 0, 0, x_hi_ready, x_lo_ready, first=True, evicted=s_evicted)
            use_tile(LIN, 1, 1, x_hi_ready, x_lo_ready)
            with pe.Fori(1, KT // 2 - 1) as pair_no:
                k0 = pair_no * 2
                for i in range(2):
                    use_tile(LIN, k0 + i, i, x_hi_ready, x_lo_ready)
            use_tile(LIN, KT - 2, 0, x_hi_ready, x_lo_ready)
            use_tile(LIN, KT - 1, 1, x_hi_ready, x_lo_ready, last=True, summed=lin_summed)

            use_tile(SQ, 0, 0, x2_hi_ready, x2_lo_ready, first=True, evicted=lin_evicted)
            use_tile(SQ, 1, 1, x2_hi_ready, x2_lo_ready)
            with pe.Fori(1, KT // 2 - 1) as pair_no:
                k0 = pair_no * 2
                for i in range(2):
                    use_tile(SQ, k0 + i, i, x2_hi_ready, x2_lo_ready)
            for h in range(H):
                for d in range(DT):
                    for k in (KT - 2, KT - 1):
                        slot = k % 2
                        if (h, d) == (0, 0):
                            pe.wait_ge(sta_hi_ready, SQ * KT + k + 1)
                            pe.wait_ge(sta_lo_ready, SQ * KT + k + 1)
                            pe.wait_ge(x2_hi_ready, k + 1)
                            pe.wait_ge(x2_lo_ready, k + 1)
                        product(h * DT + d, d, sta_hi, slot, mov_hi, k * H + h, False, False)
                        product(h * DT + d, d, sta_hi, slot, mov_lo, k * H + h, False, False)
                        mm = product(h * DT + d, d, sta_lo, slot, mov_hi, k * H + h, False, k == KT - 1)
                    mm.then_inc(q_summed, 1)

            def mlp_layer(h, w_at, in_at, in_hi, in_lo, bank_free, summed):
                for o in range(DT):
                    j = h * DT + o
                    pe.wait_ge(bank_free, j + 1)
                    for d in range(DT):
                        if o == 0:
                            pe.wait_ge(in_hi, h * DT + d + 1)
                            pe.wait_ge(in_lo, h * DT + d + 1)
                        at = in_at + h * DT + d
                        for n, (w, m) in enumerate(((mov_hi, mov_hi), (mov_hi, mov_lo), (mov_lo, mov_hi))):
                            mm = nc.tensor.matmul(psum[:, j, :], w[:, w_at + d, o * P:(o + 1) * P], m[:, at, :],
                                                  start=(d == 0 and n == 0), stop=(d == DT - 1 and n == 2))
                    mm.then_inc(summed, 1)

            pe.wait_ge(w1_hi_ready, 1)
            pe.wait_ge(w1_lo_ready, 1)
            for h in range(H):
                mlp_layer(h, W1_AT, U_AT, u_hi_ready, u_lo_ready, u_ready, mlp1_summed)
            pe.wait_ge(w2_hi_ready, 1)
            pe.wait_ge(w2_lo_ready, 1)
            for h in range(H):
                mlp_layer(h, W2_AT, HID_AT, hid_hi_ready, hid_lo_ready, hid_hi_ready, mlp2_summed)

        @block.scalar
        def _(eng):
            def sta_leading(p, k, slot, wait=True):
                eng.wait_ge(sta_loaded[slot], loads(k, slot) + p * KT * 8)
                if wait:
                    eng.wait_ge(tile_done, k + (p * KT - 1))
                nc.scalar.copy(sta_hi[:, slot, :], sta_raw[:, slot, :]).then_inc(sta_hi_ready, 1)

            def squares(k, slot, reused=True):
                eng.wait_ge(mov_loaded[slot], loads(k, slot) + KT * 8)
                eng.wait_ge(tile_done, k + (KT + 1))
                if reused:
                    eng.wait_ge(x2_lo_ready, k - 1)
                nc.scalar.activation(mov_sq[:, slot, :], mov_raw[:, slot, :], ACT.Square).then_inc(x2_ready, 1)
                nc.scalar.activation(pair(mov_hi, k), mov_raw[:, slot, :].rearrange("p (h n) -> p h n", h=H),
                                     ACT.Square).then_inc(x2_hi_ready, 1)
                eng.wait_ge(sta_loaded[slot], loads(k, slot) + SQ * KT * 8)
                if reused:
                    eng.wait_ge(sta_lo_ready, k + (SQ * KT - 1))
                nc.scalar.activation(sta_sq[:, slot, :], sta_raw[:, slot, :], ACT.Square).then_inc(e2_ready, 1)
                eng.wait_ge(tile_done, k + (SQ * KT - 1))
                nc.scalar.activation(sta_hi[:, slot, :], sta_raw[:, slot, :], ACT.Square
                                     ).then_inc(sta_hi_ready, 1)

            for k in range(2):
                sta_leading(EMB, k, k, wait=False)
            with eng.Fori(1, KT // 2) as pair_no:
                k0 = pair_no * 2
                for i in range(2):
                    sta_leading(EMB, k0 + i, i)
            sta_leading(LIN, 0, 0)
            for n in range(BANKS):
                d, h = divmod(n, H)
                if n < BANKS - 1:
                    eng.wait_ge(s_summed, n + 1)
                else:
                    eng.wait_ge(tile_done, KT)
                nc.scalar.activation(act[:, h * DT + d, :], psum[:, h * DT + d, :], ACT.Square
                                     ).then_inc(s_evicted, 1)
            sta_leading(LIN, 1, 1)
            with eng.Fori(1, KT // 2) as pair_no:
                k0 = pair_no * 2
                for i in range(2):
                    sta_leading(LIN, k0 + i, i)
            for k in range(2):
                squares(k, k, reused=False)
            with eng.Fori(1, KT // 2 - 1) as pair_no:
                k0 = pair_no * 2
                for i in range(2):
                    squares(k0 + i, i)
            eng.wait_ge(w1_loaded, 16)
            nc.scalar.copy(mov_hi[:, W1_AT:W1_AT + DT, :], w_raw[:]).then_inc(w1_hi_ready, 1)
            for k in (KT - 2, KT - 1):
                squares(k, k % 2)
            with eng.Fori(0, BANKS, 1) as j:
                eng.wait_ge(u_ready, j + 1)
                nc.scalar.copy(mov_hi[:, bass.ds(j + U_AT, 1), :], act[:, bass.ds(j, 1), :]).then_inc(u_hi_ready, 1)
            eng.wait_ge(w2_loaded, 16)
            nc.scalar.copy(mov_hi[:, W2_AT:W2_AT + DT, :], w_raw[:]).then_inc(w2_hi_ready, 1)
            eng.wait_ge(b_loaded, 16)
            with eng.Fori(0, H) as half:
                j0 = half * DT
                for o in range(DT):
                    eng.wait_ge(mlp1_summed, j0 + (o + 1))
                    nc.scalar.activation(act[:, bass.ds(j0 + o, 1), :], psum[:, bass.ds(j0 + o, 1), :], ACT.Relu,
                                         bias=b_sb[:, 1, o:o + 1], scale=0.5).then_inc(hid_ready, 1)
                    nc.scalar.activation(mov_hi[:, bass.ds(j0 + (HID_AT + o), 1), :],
                                         psum[:, bass.ds(j0 + o, 1), :], ACT.Relu,
                                         bias=b_sb[:, 1, o:o + 1], scale=0.5).then_inc(hid_hi_ready, 1)

        @block.vector
        def _(dve):
            def sta_rest(p, k, slot, src, wait=True):
                dve.wait_ge(sta_hi_ready, k + (p * KT + 1))
                if p == SQ:
                    dve.wait_ge(e2_ready, k + 1)
                if wait:
                    dve.wait_ge(tile_done, k + (p * KT - 1))
                nc.vector.tensor_tensor(sta_lo[:, slot, :], src[:, slot, :], sta_hi[:, slot, :].bitcast(F32),
                                        ALU.subtract).then_inc(sta_lo_ready, 1)

            def split_x(k, slot, wait=True):
                dve.wait_ge(mov_loaded[slot], loads(k, slot))
                raw = mov_raw[:, slot, :].rearrange("p (h n) -> p h n", h=H)
                nc.vector.tensor_copy(pair(mov_hi, k), raw).then_inc(x_hi_ready, 1)
                sta_rest(EMB, k, slot, sta_raw, wait)
                dve.wait_ge(x_hi_ready, k + 1)
                nc.vector.tensor_tensor(pair(mov_lo, k), raw, pair(mov_hi, k).bitcast(F32),
                                        ALU.subtract).then_inc(x_lo_ready, 1)

            def x2_rest(k, slot):
                dve.wait_ge(x2_ready, k + 1)
                dve.wait_ge(x2_hi_ready, k + 1)
                nc.vector.tensor_tensor(pair(mov_lo, k), mov_sq[:, slot, :].rearrange("p (h n) -> p h n", h=H),
                                        pair(mov_hi, k).bitcast(F32), ALU.subtract).then_inc(x2_lo_ready, 1)

            for k in range(2):
                split_x(k, k, wait=False)
            with dve.Fori(1, KT // 2) as pair_no:
                k0 = pair_no * 2
                for i in range(2):
                    split_x(k0 + i, i)
            with dve.Fori(0, KT // 2) as pair_no:
                k0 = pair_no * 2
                for i in range(2):
                    sta_rest(LIN, k0 + i, i, sta_raw)
            x2_rest(0, 0)
            sta_rest(SQ, 0, 0, sta_sq)
            dve.wait_ge(b_loaded, 16)
            for n in range(BANKS):
                d, h = divmod(n, H)
                if n < BANKS - 1:
                    dve.wait_ge(lin_summed, n + 1)
                else:
                    dve.wait_ge(tile_done, 2 * KT)
                nc.vector.tensor_scalar(lin[:, h * DT + d, :], psum[:, h * DT + d, :], b_sb[:, 0, d:d + 1], None,
                                        ALU.add).then_inc(lin_evicted, 1)
            x2_rest(1, 1)
            sta_rest(SQ, 1, 1, sta_sq)
            with dve.Fori(1, KT // 2 - 1) as pair_no:
                k0 = pair_no * 2
                for i in range(2):
                    x2_rest(k0 + i, i)
                    sta_rest(SQ, k0 + i, i, sta_sq)
            dve.wait_ge(w1_hi_ready, 1)
            nc.vector.tensor_tensor(mov_lo[:, W1_AT:W1_AT + DT, :], w_raw[:],
                                    mov_hi[:, W1_AT:W1_AT + DT, :].bitcast(F32), ALU.subtract
                                    ).then_inc(w1_lo_ready, 1)
            for k in (KT - 2, KT - 1):
                x2_rest(k, k % 2)
                sta_rest(SQ, k, k % 2, sta_sq)
            with dve.Fori(0, H) as half:
                j0 = half * DT
                for d in range(DT):
                    dve.wait_ge(q_summed, j0 + (d + 1))
                    bank = bass.ds(j0 + d, 1)
                    nc.vector.tensor_tensor(act[:, bank, :], act[:, bank, :], psum[:, bank, :], ALU.subtract
                                            ).then_inc(u_ready, 1)
                for d in range(DT):
                    dve.wait_ge(u_hi_ready, j0 + (d + 1))
                    at = bass.ds(j0 + (U_AT + d), 1)
                    nc.vector.tensor_tensor(mov_lo[:, at, :], act[:, bass.ds(j0 + d, 1), :],
                                            mov_hi[:, at, :].bitcast(F32), ALU.subtract).then_inc(u_lo_ready, 1)
            dve.wait_ge(w2_hi_ready, 1)
            nc.vector.tensor_tensor(mov_lo[:, W2_AT:W2_AT + DT, :], w_raw[:],
                                    mov_hi[:, W2_AT:W2_AT + DT, :].bitcast(F32), ALU.subtract
                                    ).then_inc(w2_lo_ready, 1)
            with dve.Fori(0, BANKS, 1) as j:
                dve.wait_ge(hid_ready, j + 1)
                dve.wait_ge(hid_hi_ready, j + 1)
                at = bass.ds(j + HID_AT, 1)
                nc.vector.tensor_tensor(mov_lo[:, at, :], act[:, bass.ds(j, 1), :],
                                        mov_hi[:, at, :].bitcast(F32), ALU.subtract).then_inc(hid_lo_ready, 1)
            for j in range(BANKS):
                dve.wait_ge(mlp2_summed, j + 1)
                nc.vector.scalar_tensor_tensor(out=lin[:, j, :], in0=psum[:, j, :],
                                               scalar=b_sb[:, 2, j % DT:j % DT + 1], in1=lin[:, j, :],
                                               op0=ALU.add, op1=ALU.add).then_inc(y_ready, 1)


def kernel(r_sae_features, L0_rec_emb, L0_rec_linear_w, L0_rec_linear_b, L0_rec_mlp1_w, L0_rec_mlp1_b,
           L0_rec_mlp2_w, L0_rec_mlp2_b):
    import numpy as np
    import concourse.bacc as bacc
    from concourse.bass_utils import run_bass_kernel_spmd

    def tiled(a):
        a = np.ascontiguousarray(a)
        return a.reshape(a.shape[0] // P, P, a.shape[1])

    x = np.asarray(r_sae_features)
    biases = np.stack([np.asarray(b) for b in (L0_rec_linear_b, L0_rec_mlp1_b, L0_rec_mlp2_b)])
    O = biases.shape[1]
    arrays = {
        "xT": tiled(x.T),
        "emb": tiled(np.asarray(L0_rec_emb)),
        "linT": tiled(np.asarray(L0_rec_linear_w).T),
        "w1T": tiled(np.asarray(L0_rec_mlp1_w).T),
        "w2T": tiled(np.asarray(L0_rec_mlp2_w).T),
        "bias": np.ascontiguousarray(biases.reshape(3, O // P, P).transpose(2, 0, 1)),
    }
    nc = bacc.Bacc("TRN2", target_bir_lowering=False, num_devices=1)
    ins = [nc.dram_tensor(n, a.shape, mybir.dt.from_np(a.dtype), kind="ExternalInput").ap() for n, a in arrays.items()]
    outT = nc.dram_tensor("outT", (O // P, P, x.shape[0]), F32, kind="ExternalOutput").ap()
    build(nc, *ins, outT)
    r = run_bass_kernel_spmd(nc, [arrays], core_ids=[0])
    return np.ascontiguousarray(r.results[0]["outT"].reshape(O, x.shape[0]).T)
```
